# Optimizing a Trainium2 kernel written in Bass

```python
import numpy as np
import jax
import jax.numpy as jnp

def _softmax(x, axis=-1):
    return jax.nn.softmax(x, axis=axis)

def _gelu(x):
    return jax.nn.gelu(x, approximate=True)

def _silu(x):
    return jax.nn.silu(x)

def _sigmoid(x):
    return jax.nn.sigmoid(x)

def _layernorm(x, axis=-1, eps=1e-05):
    m = jnp.mean(x, axis=axis, keepdims=True)
    v = jnp.var(x, axis=axis, keepdims=True)
    return (x - m) / jnp.sqrt(v + eps)

def _scatter_add(tgt, idx, src, axis=0):
    return tgt.at[idx].add(src)

def _segment_sum(src, seg, n):
    return jax.ops.segment_sum(src, seg, n)
kernel_name = 'mk_dlrm_tower_d1_rec_r8_aaf8be'

def setup_inputs(seed: int=0):
    np.random.seed(seed)
    _w = jnp.asarray

    def _rec_inputs():
        import jax
        import jax.numpy as jnp
        _tk = jax.random.key(seed)
        ids = jnp.stack([jax.random.randint(jax.random.fold_in(_tk, 200 + f), (512,), 0, v, jnp.int32) for f, v in enumerate([1000, 1250, 125000, 12500, 12500, 1000, 1000, 12500, 12500, 1250, 12500, 1250, 12500, 1250, 1250, 1250, 1000, 1000, 1250, 1250, 12500, 1000, 1250, 1250, 12500, 1250])], axis=1)
        tbl_0 = 0.05 * jax.random.normal(jax.random.fold_in(_tk, 500 + 0), (1000, 128), jnp.float32)
        tbl_1 = 0.05 * jax.random.normal(jax.random.fold_in(_tk, 500 + 1), (1250, 128), jnp.float32)
        tbl_2 = 0.05 * jax.random.normal(jax.random.fold_in(_tk, 500 + 2), (125000, 128), jnp.float32)
        tbl_3 = 0.05 * jax.random.normal(jax.random.fold_in(_tk, 500 + 3), (12500, 128), jnp.float32)
        tbl_4 = 0.05 * jax.random.normal(jax.random.fold_in(_tk, 500 + 4), (12500, 128), jnp.float32)
        tbl_5 = 0.05 * jax.random.normal(jax.random.fold_in(_tk, 500 + 5), (1000, 128), jnp.float32)
        tbl_6 = 0.05 * jax.random.normal(jax.random.fold_in(_tk, 500 + 6), (1000, 128), jnp.float32)
        tbl_7 = 0.05 * jax.random.normal(jax.random.fold_in(_tk, 500 + 7), (12500, 128), jnp.float32)
        tbl_8 = 0.05 * jax.random.normal(jax.random.fold_in(_tk, 500 + 8), (12500, 128), jnp.float32)
        tbl_9 = 0.05 * jax.random.normal(jax.random.fold_in(_tk, 500 + 9), (1250, 128), jnp.float32)
        tbl_10 = 0.05 * jax.random.normal(jax.random.fold_in(_tk, 500 + 10), (12500, 128), jnp.float32)
        tbl_11 = 0.05 * jax.random.normal(jax.random.fold_in(_tk, 500 + 11), (1250, 128), jnp.float32)
        tbl_12 = 0.05 * jax.random.normal(jax.random.fold_in(_tk, 500 + 12), (12500, 128), jnp.float32)
        tbl_13 = 0.05 * jax.random.normal(jax.random.fold_in(_tk, 500 + 13), (1250, 128), jnp.float32)
        tbl_14 = 0.05 * jax.random.normal(jax.random.fold_in(_tk, 500 + 14), (1250, 128), jnp.float32)
        tbl_15 = 0.05 * jax.random.normal(jax.random.fold_in(_tk, 500 + 15), (1250, 128), jnp.float32)
        tbl_16 = 0.05 * jax.random.normal(jax.random.fold_in(_tk, 500 + 16), (1000, 128), jnp.float32)
        tbl_17 = 0.05 * jax.random.normal(jax.random.fold_in(_tk, 500 + 17), (1000, 128), jnp.float32)
        tbl_18 = 0.05 * jax.random.normal(jax.random.fold_in(_tk, 500 + 18), (1250, 128), jnp.float32)
        tbl_19 = 0.05 * jax.random.normal(jax.random.fold_in(_tk, 500 + 19), (1250, 128), jnp.float32)
        tbl_20 = 0.05 * jax.random.normal(jax.random.fold_in(_tk, 500 + 20), (12500, 128), jnp.float32)
        tbl_21 = 0.05 * jax.random.normal(jax.random.fold_in(_tk, 500 + 21), (1000, 128), jnp.float32)
        tbl_22 = 0.05 * jax.random.normal(jax.random.fold_in(_tk, 500 + 22), (1250, 128), jnp.float32)
        tbl_23 = 0.05 * jax.random.normal(jax.random.fold_in(_tk, 500 + 23), (1250, 128), jnp.float32)
        tbl_24 = 0.05 * jax.random.normal(jax.random.fold_in(_tk, 500 + 24), (12500, 128), jnp.float32)
        tbl_25 = 0.05 * jax.random.normal(jax.random.fold_in(_tk, 500 + 25), (1250, 128), jnp.float32)
        _rk = jax.random.fold_in(_tk, 7)
        r_bottom_output = -0.000520686 + 1.00062 * jax.random.normal(jax.random.fold_in(_rk, 101), (512, 128), jnp.float32)
        W_top1 = 0.0456912 * jax.random.normal(jax.random.fold_in(_tk, 801), (479, 512), jnp.float32)
        W_top2 = 0.0441942 * jax.random.normal(jax.random.fold_in(_tk, 802), (512, 256), jnp.float32)
        W_top3 = 0.0625 * jax.random.normal(jax.random.fold_in(_tk, 803), (256, 1), jnp.float32)
        b_top1 = jnp.zeros((512,), jnp.float32)
        b_top2 = jnp.zeros((256,), jnp.float32)
        return (r_bottom_output, ids, tbl_0, tbl_1, tbl_2, tbl_3, tbl_4, tbl_5, tbl_6, tbl_7, tbl_8, tbl_9, tbl_10, tbl_11, tbl_12, tbl_13, tbl_14, tbl_15, tbl_16, tbl_17, tbl_18, tbl_19, tbl_20, tbl_21, tbl_22, tbl_23, tbl_24, tbl_25, W_top1, b_top1, W_top2, b_top2, W_top3)
    r_bottom_output, ids, tbl_0, tbl_1, tbl_2, tbl_3, tbl_4, tbl_5, tbl_6, tbl_7, tbl_8, tbl_9, tbl_10, tbl_11, tbl_12, tbl_13, tbl_14, tbl_15, tbl_16, tbl_17, tbl_18, tbl_19, tbl_20, tbl_21, tbl_22, tbl_23, tbl_24, tbl_25, W_top1, b_top1, W_top2, b_top2, W_top3 = _rec_inputs()

    def _L0_rec_setup():
        import jax, jax.numpy as jnp
        import numpy as np
        NUM_FEATURES = 27
        _TRIU_I, _TRIU_J = np.triu_indices(NUM_FEATURES, k=1)
        key = jax.random.key(seed)
        k1, k2 = jax.random.split(key)
        bottom_output = jax.random.normal(k1, (2048, 128), dtype=jnp.float32)
        embeddings = jax.random.normal(k2, (2048, 26, 128), dtype=jnp.float32)
        return {'bottom_output': bottom_output, 'embeddings': embeddings}
    _L0_rec_all = _L0_rec_setup()
    _L0_rec_in = {k: v for k, v in _L0_rec_all.items() if k in ()}
    del _L0_rec_all
    return {'r_bottom_output': r_bottom_output, 'ids': ids, 'tbl_0': tbl_0, 'tbl_1': tbl_1, 'tbl_2': tbl_2, 'tbl_3': tbl_3, 'tbl_4': tbl_4, 'tbl_5': tbl_5, 'tbl_6': tbl_6, 'tbl_7': tbl_7, 'tbl_8': tbl_8, 'tbl_9': tbl_9, 'tbl_10': tbl_10, 'tbl_11': tbl_11, 'tbl_12': tbl_12, 'tbl_13': tbl_13, 'tbl_14': tbl_14, 'tbl_15': tbl_15, 'tbl_16': tbl_16, 'tbl_17': tbl_17, 'tbl_18': tbl_18, 'tbl_19': tbl_19, 'tbl_20': tbl_20, 'tbl_21': tbl_21, 'tbl_22': tbl_22, 'tbl_23': tbl_23, 'tbl_24': tbl_24, 'tbl_25': tbl_25, 'W_top1': W_top1, 'b_top1': b_top1, 'W_top2': W_top2, 'b_top2': b_top2, 'W_top3': W_top3}

def reference(r_bottom_output, ids, tbl_0, tbl_1, tbl_2, tbl_3, tbl_4, tbl_5, tbl_6, tbl_7, tbl_8, tbl_9, tbl_10, tbl_11, tbl_12, tbl_13, tbl_14, tbl_15, tbl_16, tbl_17, tbl_18, tbl_19, tbl_20, tbl_21, tbl_22, tbl_23, tbl_24, tbl_25, W_top1, b_top1, W_top2, b_top2, W_top3):
    import jax
    import jax.numpy as jnp

    def _L0_rec_ref(bottom_output, embeddings):
        import jax, jax.numpy as jnp
        import numpy as np
        NUM_FEATURES = 27
        _TRIU_I, _TRIU_J = np.triu_indices(NUM_FEATURES, k=1)
        all_emb = jnp.concatenate([bottom_output[:, None, :], embeddings], axis=1)
        gram = jnp.einsum('bfd,bgd->bfg', all_emb, all_emb)
        return gram[:, _TRIU_I, _TRIU_J]
    e = jnp.stack([tbl_0[ids[:, 0]], tbl_1[ids[:, 1]], tbl_2[ids[:, 2]], tbl_3[ids[:, 3]], tbl_4[ids[:, 4]], tbl_5[ids[:, 5]], tbl_6[ids[:, 6]], tbl_7[ids[:, 7]], tbl_8[ids[:, 8]], tbl_9[ids[:, 9]], tbl_10[ids[:, 10]], tbl_11[ids[:, 11]], tbl_12[ids[:, 12]], tbl_13[ids[:, 13]], tbl_14[ids[:, 14]], tbl_15[ids[:, 15]], tbl_16[ids[:, 16]], tbl_17[ids[:, 17]], tbl_18[ids[:, 18]], tbl_19[ids[:, 19]], tbl_20[ids[:, 20]], tbl_21[ids[:, 21]], tbl_22[ids[:, 22]], tbl_23[ids[:, 23]], tbl_24[ids[:, 24]], tbl_25[ids[:, 25]]], axis=1)
    z = _L0_rec_ref(r_bottom_output, e)
    z = z.reshape(z.shape[0], -1)
    h = jnp.concatenate([z, r_bottom_output], axis=1)
    h = jnp.maximum(h @ W_top1 + b_top1, 0.0)
    h = jnp.maximum(h @ W_top2 + b_top2, 0.0)
    y = h @ W_top3
    return y

_drawn_inputs = setup_inputs


def setup_inputs(seed=0):
    import zlib

    import numpy as np

    out = dict(_drawn_inputs(seed))
    spreads = {'b_top1': (0.0, 0.1), 'b_top2': (0.0, 0.1)}
    factors = {}
    for name, (base, spread) in spreads.items():
        noise = np.random.default_rng([zlib.crc32(name.encode()), seed]).standard_normal(out[name].shape)
        drawn = base * np.exp(spread * noise) if base else spread * noise
        out[name] = jnp.asarray(drawn.astype(out[name].dtype))
    for name, factor in factors.items():
        out[name] = (out[name] * factor).astype(out[name].dtype)
    return out
```

```python
from contextlib import ExitStack

import numpy as np
import concourse.bass as bass
from concourse import mybir

F32 = mybir.dt.float32
I32 = mybir.dt.int32
ALU = mybir.AluOpType
ACT = mybir.ActivationFunctionType

P = 128
BATCH = 512
TILES = BATCH // P
TABLES = 26
FEATURES = TABLES + 1
SLOTS = 32
QUAD = 4
QUADS = P // QUAD
SPAN = 13
OTHERS = FEATURES - 1
ROWS = SLOTS * OTHERS

GROUP = 4
GROUPS = [range(g, min(g + GROUP, FEATURES)) for g in range(0, FEATURES, GROUP)]

BANK = 512
RUN = 2 * BANK // P
RUNS = QUADS // RUN

HIDDEN1, HIDDEN2 = 512, 256

PER_CHUNK = 4
BLOCKS = [(0, OTHERS * i, i, OTHERS, 3, PER_CHUNK, FEATURES) for i in range(PER_CHUNK)]
SPARE = P - PER_CHUNK * OTHERS
BLOCKS += [(0, PER_CHUNK * OTHERS, SPAN - 1, SPARE, 1, 0, FEATURES),
           (1, PER_CHUNK * OTHERS, SPAN - 1 + SPARE * FEATURES, OTHERS - SPARE, 1, 0, FEATURES),
           (2, PER_CHUNK * OTHERS, SPAN, SPAN, 1, 0, 1)]
CHUNK_ROWS = [P, PER_CHUNK * OTHERS + OTHERS - SPARE, PER_CHUNK * OTHERS + SPAN]
PAIR_CHUNKS = len(CHUNK_ROWS)
CHUNK_START = [sum(CHUNK_ROWS[:c]) for c in range(PAIR_CHUNKS + 1)]
PAIRS = CHUNK_START[-1]

BATCHES = [(0, 3), (3, 4)]


def pair_order():
    number = {}
    for f in range(FEATURES):
        for g in range(f + 1, FEATURES):
            number[f, g] = len(number)
    order = np.zeros(PAIRS, np.int64)
    for chunk, part, row, rows, chunks, chunk_step, step in BLOCKS:
        for c in range(chunks):
            for r in range(rows):
                f, g = divmod(row + c * chunk_step + r * step, OTHERS)
                order[CHUNK_START[chunk + c] + part + r] = number[min(f, g + 1), max(f, g + 1)]
    assert sorted(order) == list(range(len(number)))
    return order


def dlrm_tower(nc, dense, ids, tables, w1, b1, w2, b2, w3, out):
    with ExitStack() as ctx:
        def sb(name, shape, dt=F32):
            return ctx.enter_context(nc.sbuf_tensor(name, shape, dt))

        def psum(name, shape):
            return ctx.enter_context(nc.psum_tensor(name, shape, F32))

        def sem(name):
            return ctx.enter_context(nc.semaphore(name))

        ids_sb = sb("ids_sb", [P, TILES, TABLES], I32)
        identity = sb("identity", [P, P])
        dense_sb = sb("dense_sb", [P, TILES, P])
        rows_sb = sb("rows_sb", [P, TILES, TABLES, P])
        turned = sb("turned", [P, TILES, QUADS, QUAD, SLOTS])
        dense_turned = sb("dense_turned", [P, BATCH])
        products = sb("products", [P, TILES, OTHERS, QUADS])
        pairs = sb("pairs", [P, PAIR_CHUNKS, BATCH])
        w1_sb = sb("w1_sb", [P, PAIR_CHUNKS + 1, HIDDEN1])
        w2_sb = sb("w2_sb", [P, HIDDEN1 // P, HIDDEN2])
        w3_sb = sb("w3_sb", [P, HIDDEN2 // P])
        b1_sb = sb("b1_sb", [P, HIDDEN1 // P])
        b2_sb = sb("b2_sb", [P, HIDDEN2 // P])
        hidden1 = sb("hidden1", [P, HIDDEN1 // P, BATCH])
        hidden2 = sb("hidden2", [P, HIDDEN2 // P, BATCH])
        y_sb = sb("y_sb", [1, BATCH])
        products_dram = nc.dram_tensor("products_dram", (TILES, ROWS, P), F32, kind="Internal").ap()

        turn_ps = psum("turn_ps", [P, 2, GROUP, P])
        product_ps = psum("product_ps", [P, 2, RUN, P])
        layer_ps = psum("layer_ps", [P, 2, BANK])

        ids_in = sem("ids_in")
        dense_in = sem("dense_in")
        w1_in, w2_in, small_in = sem("w1_in"), sem("w2_in"), sem("small_in")
        ones_set, identity_set, padding_set = sem("ones_set"), sem("identity_set"), sem("padding_set")
        gathered = [[sem(f"gathered_{t}_{g}") for g in range(len(GROUPS))] for t in range(TILES)]
        group_turned = sem("group_turned")
        copied = [sem("copied_by_vector"), sem("copied_by_scalar")]
        run_done = sem("run_done")
        kept = [sem("kept_by_vector"), sem("kept_by_scalar")]
        stored = [sem(f"stored_{t}") for t in range(TILES)]
        pairs_in = [sem(f"pairs_in_{t}") for t in range(TILES)]
        layer_done = sem("layer_done")
        relu_done = [sem("relu_by_vector"), sem("relu_by_scalar")]
        y_done, y_stored = sem("y_done"), sem("y_stored")

        block = ctx.enter_context(nc.Block())

        n_groups = len(GROUPS)
        per_batch = HIDDEN1 // P + HIDDEN2 // P + 1

        def own(n):
            return n // 2 + 1

        @block.gpsimd
        def _(pool):
            pool.memset(identity[:], 1.0).then_inc(ones_set, 1)
            pool.wait_ge(ones_set, 1)
            pool.affine_select(out=identity[:], in_=identity[:], compare_op=ALU.is_equal, fill=0.0, base=0,
                               pattern=[[-1, P]], channel_multiplier=1).then_inc(identity_set, 1)
            pool.wait_ge(ids_in, 16)
            for t in range(TILES):
                for g, group in enumerate(GROUPS):
                    for f in group:
                        if f == 0:
                            continue
                        pool.indirect_dma_start(
                            rows_sb[:, t, f - 1, :], None, tables[f - 1],
                            bass.IndirectOffsetOnAxis(ap=ids_sb[:, t, f - 1:f], axis=0),
                        ).then_inc(gathered[t][g], 16)

        def load_pairs(eng, t, blocks):
            for chunk, part, row, rows, chunks, chunk_step, step in blocks:
                src = products_dram[t, row:row + (rows - 1) * step + (chunks - 1) * chunk_step + 1, :]
                src = bass.AP(products_dram.tensor, (t * ROWS + row) * P,
                              [[step * P, rows], [chunk_step * P, chunks], [1, P]])
                eng.dma_start(pairs[part:part + rows, chunk:chunk + chunks, t * P:(t + 1) * P],
                              src).then_inc(pairs_in[t], 16)

        def store_products(eng, t, j):
            eng.dma_start(
                products_dram[t, :, j * QUADS:(j + 1) * QUADS].rearrange("(f g) q -> f g q", g=OTHERS),
                products[j * SLOTS:(j + 1) * SLOTS, t, :, :]).then_inc(stored[t], 16)

        @block.sync
        def _(sp):
            sp.dma_start(ids_sb[:], ids.rearrange("(t p) f -> p t f", p=P)).then_inc(ids_in, 16)
            sp.dma_start(dense_sb[:], dense.rearrange("(t p) d -> p t d", p=P)).then_inc(dense_in, 16)
            for c, rows in enumerate(CHUNK_ROWS + [P]):
                start = sum(CHUNK_ROWS[:c])
                sp.dma_start(w1_sb[0:rows, c, :], w1[start:start + rows, :]).then_inc(w1_in, 16)
            sp.dma_start(w2_sb[:], w2.rearrange("(c p) n -> p c n", p=P)).then_inc(w2_in, 16)
            sp.dma_start(w3_sb[:], w3).then_inc(small_in, 16)
            sp.dma_start(b1_sb[:], b1).then_inc(small_in, 16)
            sp.dma_start(b2_sb[:], b2).then_inc(small_in, 16)
            for t in range(TILES):
                sp.wait_ge(kept[0], 2 * RUNS * (t + 1))
                for j in range(2):
                    store_products(sp, t, j)
                sp.wait_ge(kept[1], 2 * RUNS * (t + 1))
                for j in range(2, 4):
                    store_products(sp, t, j)
                sp.wait_ge(stored[t], 16 * QUAD)
                load_pairs(sp, t, BLOCKS)
            sp.wait_ge(y_done, len(BATCHES))
            sp.dma_start(out, y_sb[:]).then_inc(y_stored, 16)
            sp.wait_ge(y_stored, 16)

        @block.tensor
        def _(pe):
            def turn_groups(t):
                for g, group in enumerate(GROUPS):
                    n = t * n_groups + g
                    pe.wait_ge(gathered[t][g], 16 * sum(f > 0 for f in group))
                    if n >= 2:
                        pe.wait_ge(copied[n % 2], own(n - 2))
                    for k, f in enumerate(group):
                        src = dense_sb[:, t, :] if f == 0 else rows_sb[:, t, f - 1, :]
                        last = pe.transpose(turn_ps[:, n % 2, k, :], src, identity[:])
                    last.then_inc(group_turned, 1)

            def multiply_features(t):
                n = t * n_groups + n_groups - 1
                for m in (n - 1, n):
                    pe.wait_ge(copied[m % 2], own(m))
                for r in range(RUNS):
                    m = t * RUNS + r
                    if m >= 2:
                        for keeper in kept:
                            pe.wait_ge(keeper, 2 * (m - 1))
                    for k in range(RUN):
                        q = r * RUN + k
                        last = pe.matmul(
                            product_ps[:, m % 2, k, 0:QUAD * OTHERS],
                            turned[:, t, q, :, :].rearrange("p j f -> p (j f)"),
                            turned[:, t, q, :, 1:FEATURES], start=True, stop=True)
                    last.then_inc(run_done, 1)

            def dense_layers(b):
                t0, t1 = BATCHES[b]
                s, e = t0 * P, t1 * P
                n = b * per_batch
                for t in range(t0, t1):
                    pe.wait_ge(pairs_in[t], 16 * len(BLOCKS))
                for h in range(HIDDEN1 // P):
                    if n >= 2:
                        pe.wait_ge(relu_done[n % 2], own(n - 2))
                    for c, rows in enumerate(CHUNK_ROWS + [P]):
                        rhs = pairs[0:rows, c, s:e] if c < PAIR_CHUNKS else dense_turned[:, s:e]
                        last = pe.matmul(layer_ps[:, n % 2, 0:e - s], w1_sb[0:rows, c, h * P:(h + 1) * P], rhs,
                                         start=(c == 0), stop=(c == PAIR_CHUNKS))
                    last.then_inc(layer_done, 1)
                    n += 1
                pe.wait_ge(w2_in, 16)
                for h in range(HIDDEN2 // P):
                    pe.wait_ge(relu_done[n % 2], own(n - 2))
                    for c in range(HIDDEN1 // P):
                        if h == 0:
                            m = b * per_batch + c
                            pe.wait_ge(relu_done[m % 2], own(m))
                        last = pe.matmul(layer_ps[:, n % 2, 0:e - s], w2_sb[:, c, h * P:(h + 1) * P],
                                         hidden1[:, c, s:e], start=(c == 0), stop=(c == HIDDEN1 // P - 1))
                    last.then_inc(layer_done, 1)
                    n += 1
                pe.wait_ge(small_in, 16 * 3)
                for c in range(HIDDEN2 // P):
                    m = b * per_batch + HIDDEN1 // P + c
                    pe.wait_ge(relu_done[m % 2], own(m))
                for c in range(HIDDEN2 // P):
                    last = pe.matmul(layer_ps[0:1, n % 2, 0:e - s], w3_sb[:, c:c + 1], hidden2[:, c, s:e],
                                     start=(c == 0), stop=(c == HIDDEN2 // P - 1))
                last.then_inc(layer_done, 1)

            pe.wait_ge(identity_set, 1)
            pe.wait_ge(dense_in, 16)
            pe.wait_ge(padding_set, 1)
            for t in range(TILES):
                turn_groups(t)
                multiply_features(t)
                if t == 0:
                    pe.wait_ge(w1_in, 16 * (PAIR_CHUNKS + 1))
                for b, (_, end) in enumerate(BATCHES):
                    if end == t + 1:
                        dense_layers(b)

        def keep(copy, eng, which, t):
            for r in range(RUNS):
                m = t * RUNS + r
                eng.wait_ge(run_done, m + 1)
                for j in range(2 * which, 2 * which + 2):
                    part = slice(j * SLOTS, (j + 1) * SLOTS)
                    copy(products[part, t, :, r * RUN:(r + 1) * RUN].rearrange("p g q -> p q g"),
                         product_ps[part, m % 2, :, j * OTHERS:(j + 1) * OTHERS]).then_inc(kept[which], 1)

        def copy_groups(copy, eng, which, t):
            for g, group in enumerate(GROUPS):
                n = t * n_groups + g
                if n % 2 != which:
                    continue
                eng.wait_ge(group_turned, n + 1)
                if g == 0:
                    copy(dense_turned[:, t * P:(t + 1) * P], turn_ps[:, n % 2, 0, :])
                copy(turned[:, t, :, :, group.start:group.stop].rearrange("p q j f -> p f j q"),
                     turn_ps[:, n % 2, 0:len(group), :].rearrange("p f (j q) -> p f j q", j=QUAD)
                     ).then_inc(copied[which], 1)

        def take_layers(relu, eng, which, b):
            s, e = BATCHES[b][0] * P, BATCHES[b][1] * P
            for i in range(per_batch - 1):
                n = b * per_batch + i
                if n % 2 != which:
                    continue
                eng.wait_ge(layer_done, n + 1)
                c = i - HIDDEN1 // P
                dst, bias = (hidden1[:, i, s:e], b1_sb[:, i:i + 1]) if c < 0 else (hidden2[:, c, s:e], b2_sb[:, c:c + 1])
                relu(dst, layer_ps[:, n % 2, 0:e - s], bias).then_inc(relu_done[which], 1)
            n = b * per_batch + per_batch - 1
            if n % 2 == which:
                eng.wait_ge(layer_done, n + 1)
                return n
            return None

        @block.vector
        def _(dve):
            dve.memset(turned[:, :, :, :, FEATURES:SLOTS].rearrange("p t q j f -> p (t q j) f"), 0.0).then_inc(padding_set, 1)

            def relu(dst, src, bias):
                return dve.tensor_scalar(dst, src, bias, 0.0, ALU.add, ALU.max)

            for t in range(TILES):
                copy_groups(dve.tensor_copy, dve, 0, t)
                keep(dve.tensor_copy, dve, 0, t)
                if t == 0:
                    dve.wait_ge(small_in, 16 * 3)
                for b, (start, end) in enumerate(BATCHES):
                    if end == t + 1:
                        n = take_layers(relu, dve, 0, b)
                        if n is not None:
                            dve.tensor_copy(y_sb[:, start * P:end * P], layer_ps[0:1, n % 2, 0:(end - start) * P]
                                            ).then_inc(relu_done[0], 1)
                            dve.wait_ge(relu_done[0], own(n))
                            dve.engine_nop().then_inc(y_done, 1)

        @block.scalar
        def _(act):
            def relu(dst, src, bias):
                return act.activation(dst, src, ACT.Relu, bias=bias)

            for t in range(TILES):
                copy_groups(act.copy, act, 1, t)
                keep(act.copy, act, 1, t)
                if t == 0:
                    act.wait_ge(small_in, 16 * 3)
                for b, (start, end) in enumerate(BATCHES):
                    if end == t + 1:
                        n = take_layers(relu, act, 1, b)
                        if n is not None:
                            act.copy(y_sb[:, start * P:end * P], layer_ps[0:1, n % 2, 0:(end - start) * P]
                                     ).then_inc(relu_done[1], 1)
                            act.wait_ge(relu_done[1], own(n))
                            act.sem_inc(y_done, 1)


def kernel(**inputs):
    import numpy as np
    import concourse.bacc as bacc
    from concourse import mybir
    from concourse.bass_utils import run_bass_kernel_spmd

    nc = bacc.Bacc("TRN2", target_bir_lowering=False, num_devices=1)
    arrays = {}

    def arg(name, array):
        arrays["in_" + name] = a = np.ascontiguousarray(array)
        return nc.dram_tensor("in_" + name, a.shape, mybir.dt.from_np(a.dtype), kind="ExternalInput").ap()

    def columns(v):
        return np.asarray(v).reshape(-1, P).T

    w1 = np.asarray(inputs["W_top1"])
    w1 = np.concatenate([w1[:PAIRS][pair_order()], w1[PAIRS:]])
    out = nc.dram_tensor("out_y", (1, BATCH), F32, kind="ExternalOutput").ap()
    dlrm_tower(
        nc, arg("dense", inputs["r_bottom_output"]), arg("ids", inputs["ids"]),
        [arg(f"tbl_{f}", inputs[f"tbl_{f}"]) for f in range(TABLES)],
        arg("w1", w1), arg("b1", columns(inputs["b_top1"])),
        arg("w2", inputs["W_top2"]), arg("b2", columns(inputs["b_top2"])),
        arg("w3", columns(inputs["W_top3"])), out)
    result = run_bass_kernel_spmd(nc, [arrays], core_ids=[0])
    return np.asarray(result.results[0]["out_y"]).reshape(BATCH, 1)
```

```python
from contextlib import ExitStack

import numpy as np
import concourse.bass as bass
from concourse import mybir

F32 = mybir.dt.float32
F32R = mybir.dt.float32r
I32 = mybir.dt.int32
ALU = mybir.AluOpType
ACT = mybir.ActivationFunctionType

P = 128
BATCH = 512
TILES = BATCH // P
ROWS_OF = [1000, 1250, 125000, 12500, 12500, 1000, 1000, 12500, 12500, 1250, 12500, 1250, 12500,
           1250, 1250, 1250, 1000, 1000, 1250, 1250, 12500, 1000, 1250, 1250, 12500, 1250]
TABLES = len(ROWS_OF)
FEATURES = TABLES + 1
SLOTS = 28
QUAD = 4
QUADS = P // QUAD

MIXED_PER_SAMPLE = 16
SIDES = 2
BY_SIZE = sorted(range(TABLES), key=lambda f: ROWS_OF[f])
LOOKUP = BY_SIZE[:TABLES - MIXED_PER_SAMPLE - SIDES]
SIDE = BY_SIZE[len(LOOKUP):len(LOOKUP) + SIDES]
MIXED = BY_SIZE[len(LOOKUP) + SIDES:]
SLOT_TABLES = [None] + SIDE + LOOKUP + MIXED
FIRST_LOOKUP = 1 + SIDES
FIRST_MIXED = FIRST_LOOKUP + len(LOOKUP)

TABLE_PARTS = 125
CHUNKS_OF = [ROWS_OF[f] // TABLE_PARTS for f in LOOKUP]
MOST_CHUNKS = max(CHUNKS_OF)
CHUNK_KINDS = sorted(set(CHUNKS_OF))
FIRST_CHUNK = [sum(CHUNKS_OF[:i]) for i in range(len(LOOKUP) + 1)]
RAW_RING = 3
SCALAR_CHUNKS_OF = [1] * len(LOOKUP)
SCALAR_CHUNKS = max(SCALAR_CHUNKS_OF)
VECTOR_CHUNKS_OF = [c - s for c, s in zip(CHUNKS_OF, SCALAR_CHUNKS_OF)]
FIRST_SCALAR = [sum(SCALAR_CHUNKS_OF[:i]) for i in range(len(LOOKUP) + 1)]
FIRST_VECTOR = [sum(VECTOR_CHUNKS_OF[:i]) for i in range(len(LOOKUP) + 1)]
FIRST_START = 1 + len(CHUNK_KINDS)
ONE_HOT_RING = 4
WARM_UPS = 20

BANK = 512
BLOCK_QUADS = P // MIXED_PER_SAMPLE
BLOCKS_PER_TILE = QUADS // BLOCK_QUADS
BLOCKS = TILES * BLOCKS_PER_TILE
GATHERS = BLOCKS * QUAD

SPAN = 13
OTHERS = FEATURES - 1
ROWS = SLOTS * OTHERS

BATCHES = [(0, 1), (1, 3), (3, 4)]
BATCH_AFTER = [9, 15, 15]

HIDDEN1, HIDDEN2 = 512, 256
OUTS1, OUTS2 = HIDDEN1 // P, HIDDEN2 // P
WIDEST = max(end - start for start, end in BATCHES) * P
OUTS = OUTS1 + OUTS2 + 1

PER_CHUNK = 4
SPARE = P - PER_CHUNK * OTHERS
PAIR_LOADS = [(0, OTHERS * i, i, OTHERS, 3, PER_CHUNK, FEATURES) for i in range(PER_CHUNK)]
PAIR_LOADS += [(0, PER_CHUNK * OTHERS, SPAN - 1, SPARE, 1, 0, FEATURES),
               (1, PER_CHUNK * OTHERS, SPAN - 1 + SPARE * FEATURES, OTHERS - SPARE, 1, 0, FEATURES),
               (2, PER_CHUNK * OTHERS, SPAN, SPAN, 1, 0, 1)]
CHUNK_ROWS = [P, PER_CHUNK * OTHERS + OTHERS - SPARE, PER_CHUNK * OTHERS + SPAN]
PAIR_CHUNKS = len(CHUNK_ROWS)
CHUNK_START = [sum(CHUNK_ROWS[:c]) for c in range(PAIR_CHUNKS + 1)]
PAIRS = CHUNK_START[-1]

GROUPS_PER_TILE = 1 + BLOCKS_PER_TILE


def group_of(b):
    return b // BLOCKS_PER_TILE * GROUPS_PER_TILE + 1 + b % BLOCKS_PER_TILE


def plan():
    steps, turned = [], 0

    def turn_up_to(n):
        nonlocal turned
        while turned <= min(n, TILES * GROUPS_PER_TILE - 1):
            steps.append(("turn", turned))
            turned += 1

    for i in range(len(LOOKUP)):
        steps.append(("lookup", i))
        if i >= 2:
            turn_up_to(i - 2)
    for b in range(BLOCKS):
        turn_up_to(group_of(b + 1))
        steps.append(("multiply", b))
        steps += [("layers", i) for i, after in enumerate(BATCH_AFTER) if after == b]
    return steps


PLAN = plan()
LAST_LOOKUP = PLAN.index(("lookup", len(LOOKUP) - 1))
COPIER = [1 if PLAN.index(("turn", n)) <= LAST_LOOKUP else n % 2 for n in range(TILES * GROUPS_PER_TILE)]


def copies(n):
    return COPIER[:n + 1].count(COPIER[n])


def layer_turns(n):
    return n // 2 + 1


def pair_order():
    number = {}
    for f in range(FEATURES):
        for g in range(f + 1, FEATURES):
            number[f, g] = len(number)
    feature = [0] + [f + 1 for f in SLOT_TABLES[1:]]
    order = np.zeros(PAIRS, np.int64)
    for chunk, part, row, rows, chunks, chunk_step, step in PAIR_LOADS:
        for c in range(chunks):
            for r in range(rows):
                f, g = divmod(row + c * chunk_step + r * step, OTHERS)
                f, g = feature[f], feature[g + 1]
                order[CHUNK_START[chunk + c] + part + r] = number[min(f, g), max(f, g)]
    assert sorted(order) == list(range(len(number)))
    return order


def dlrm_tower(nc, dense, side_ids, side_tables, lookup_ids, lookup_tables, mixed_ids, mixed_table, starts,
               w1, b1, w2, b2, w3, out):
    with ExitStack() as ctx:
        def sb(name, shape, dt=F32):
            return ctx.enter_context(nc.sbuf_tensor(name, shape, dt))

        def psum(name, shape):
            return ctx.enter_context(nc.psum_tensor(name, shape, F32))

        def sem(name):
            return ctx.enter_context(nc.semaphore(name))

        starts_sb = sb("starts_sb", [P, FIRST_START + FIRST_SCALAR[-1]])
        mixed_ids_sb = sb("mixed_ids_sb", [P, GATHERS], I32)
        mixed_rows_sb = sb("mixed_rows_sb", [P, GATHERS], I32)
        side_ids_sb = sb("side_ids_sb", [P, TILES, SIDES], I32)
        lookup_ids_sb = sb("lookup_ids_sb", [P, RAW_RING, BATCH], I32)
        identity = sb("identity", [P, P])
        dense_sb = sb("dense_sb", [P, TILES, P])
        side_sb = sb("side_sb", [P, TILES, SIDES, P])
        mixed_sb = sb("mixed_sb", [P, GATHERS, P])
        raw = sb("raw", [P, RAW_RING, MOST_CHUNKS, P])
        high = sb("high", [P, 2, MOST_CHUNKS, P], F32R)
        low = sb("low", [P, 2, MOST_CHUNKS, P], F32R)
        one_hot = sb("one_hot", [P, ONE_HOT_RING, BATCH], F32R)
        scalar_one_hot = sb("scalar_one_hot", [P, 2, SCALAR_CHUNKS, BATCH], F32R)
        distance = sb("distance", [P, BATCH])
        turned = sb("turned", [P, TILES, QUADS, QUAD, SLOTS])
        dense_turned = sb("dense_turned", [P, BATCH])
        products = sb("products", [QUAD * SLOTS, 2, QUAD, OTHERS, QUADS])
        pairs = sb("pairs", [P, PAIR_CHUNKS, BATCH])
        w1_sb = sb("w1_sb", [P, PAIR_CHUNKS + 1, HIDDEN1])
        w2_sb = sb("w2_sb", [P, OUTS1, HIDDEN2])
        w3_sb = sb("w3_sb", [P, OUTS2])
        b1_sb = sb("b1_sb", [P, OUTS1])
        b2_sb = sb("b2_sb", [P, OUTS2])
        hidden1 = sb("hidden1", [P, OUTS1, WIDEST])
        hidden2 = sb("hidden2", [P, OUTS2, WIDEST])
        y_sb = sb("y_sb", [1, BATCH])
        products_dram = nc.dram_tensor("products_dram", (TILES, ROWS, P), F32, kind="Internal").ap()

        turn_ps = psum("turn_ps", [P, 2, QUAD, P])
        product_ps = psum("product_ps", [P, 2, BLOCK_QUADS, P])
        layer_ps = psum("layer_ps", [P, 2, BANK])

        starts_in, mixed_ids_in, side_ids_in = sem("starts_in"), sem("mixed_ids_in"), sem("side_ids_in")
        lookup_ids_in = [sem(f"lookup_ids_in_{i}") for i in range(len(LOOKUP))]
        table_in = [sem(f"table_in_{i}") for i in range(len(LOOKUP))]
        dense_in, w1_in, w2_in, small_in = sem("dense_in"), sem("w1_in"), sem("w2_in"), sem("small_in")
        ones_set, identity_set, padding_set = sem("ones_set"), sem("identity_set"), sem("padding_set")
        mixed_rows_set = sem("mixed_rows_set")
        side_gathered = [sem(f"side_gathered_{t}") for t in range(TILES)]
        mixed_gathered = [sem(f"mixed_gathered_{b}") for b in range(BLOCKS)]
        high_set, low_set = sem("high_set"), sem("low_set")
        one_hot_set, scalar_one_hot_set, distance_set = sem("one_hot_set"), sem("scalar_one_hot_set"), sem("distance_set")
        chunk_used = sem("chunk_used")
        lookup_copied = sem("lookup_copied")
        group_turned = sem("group_turned")
        copied = [sem("copied_by_vector"), sem("copied_by_scalar")]
        block_multiplied = sem("block_multiplied")
        kept = [sem("kept_by_vector"), sem("kept_by_scalar")]
        stored = [sem(f"stored_{t}") for t in range(TILES)]
        pairs_in = [sem(f"pairs_in_{t}") for t in range(TILES)]
        layer_done = sem("layer_done")
        layer_taken = [sem("layer_taken_by_vector"), sem("layer_taken_by_scalar")]
        y_stored = sem("y_stored")

        block = ctx.enter_context(nc.Block())

        @block.gpsimd
        def _(pool):
            pool.memset(identity[:], 1.0).then_inc(ones_set, 1)
            pool.wait_ge(ones_set, 1)
            pool.affine_select(out=identity[:], in_=identity[:], compare_op=ALU.is_equal, fill=0.0, base=0,
                               pattern=[[-1, P]], channel_multiplier=1).then_inc(identity_set, 1)
            for t in range(TILES):
                if t == 0:
                    pool.wait_ge(side_ids_in, 16)
                for i in range(SIDES):
                    pool.indirect_dma_start(
                        side_sb[:, t, i, :], None, side_tables[i],
                        bass.IndirectOffsetOnAxis(ap=side_ids_sb[:, t, i:i + 1], axis=0),
                    ).then_inc(side_gathered[t], 16)
                if t == 0:
                    pool.wait_ge(mixed_rows_set, 1)
                for b in range(t * BLOCKS_PER_TILE, (t + 1) * BLOCKS_PER_TILE):
                    for n in range(b * QUAD, (b + 1) * QUAD):
                        pool.indirect_dma_start(
                            mixed_sb[:, n, :], None, mixed_table,
                            bass.IndirectOffsetOnAxis(ap=mixed_rows_sb[:, n:n + 1], axis=0),
                        ).then_inc(mixed_gathered[b], 16)

        @block.sync
        def _(sp):
            def load_table(i):
                sp.dma_start(raw[0:TABLE_PARTS, i % RAW_RING, 0:CHUNKS_OF[i], :].rearrange("p c d -> p (c d)"),
                             lookup_tables[i].rearrange("(p c) d -> p (c d)", p=TABLE_PARTS)
                             ).then_inc(table_in[i], 16)

            def load_lookup_ids(i):
                sp.dma_start(lookup_ids_sb[:, i % RAW_RING, :], lookup_ids[i:i + 1, :].to_broadcast([P, BATCH])
                             ).then_inc(lookup_ids_in[i], 16)

            sp.dma_start(side_ids_sb[:].rearrange("p t i -> p (t i)"), side_ids).then_inc(side_ids_in, 16)
            load_table(0)
            load_lookup_ids(0)
            sp.dma_start(dense_sb[:], dense.rearrange("(t p) d -> p t d", p=P)).then_inc(dense_in, 16)
            for i in range(1, RAW_RING):
                load_table(i)
                load_lookup_ids(i)
            for i in range(RAW_RING, len(LOOKUP)):
                sp.wait_ge(high_set, i - RAW_RING + 1)
                sp.wait_ge(low_set, i - RAW_RING + 1)
                load_table(i)
                sp.wait_ge(one_hot_set, FIRST_VECTOR[i - RAW_RING + 1])
                sp.wait_ge(distance_set, FIRST_SCALAR[i - RAW_RING + 1])
                load_lookup_ids(i)
            for c, rows in enumerate(CHUNK_ROWS + [P]):
                start = sum(CHUNK_ROWS[:c])
                sp.dma_start(w1_sb[0:rows, c, :], w1[start:start + rows, :]).then_inc(w1_in, 16)
            sp.dma_start(w2_sb[:], w2.rearrange("(c p) n -> p c n", p=P)).then_inc(w2_in, 16)
            sp.dma_start(w3_sb[:], w3).then_inc(small_in, 16)
            sp.dma_start(b1_sb[:], b1).then_inc(small_in, 16)
            sp.dma_start(b2_sb[:], b2).then_inc(small_in, 16)
            for t in range(TILES):
                for keeper in kept:
                    sp.wait_ge(keeper, BLOCKS_PER_TILE * (t + 1))
                for j in range(QUAD):
                    sp.dma_start(
                        products_dram[t, :, j * QUADS:(j + 1) * QUADS].rearrange("(f g) q -> f g q", g=OTHERS),
                        products[j * SLOTS:(j + 1) * SLOTS, t % 2, j, :, :]).then_inc(stored[t], 16)
                sp.wait_ge(stored[t], 16 * QUAD)
                for chunk, part, row, rows, chunks, chunk_step, step in PAIR_LOADS:
                    sp.dma_start(pairs[part:part + rows, chunk:chunk + chunks, t * P:(t + 1) * P],
                                 bass.AP(products_dram.tensor, (t * ROWS + row) * P,
                                         [[step * P, rows], [chunk_step * P, chunks], [1, P]])
                                 ).then_inc(pairs_in[t], 16)
            for which in range(2):
                n = len(BATCHES) * OUTS - 1 - which
                sp.wait_ge(layer_taken[n % 2], layer_turns(n))
            sp.dma_start(out, y_sb[:]).then_inc(y_stored, 16)
            sp.wait_ge(y_stored, 16)

        @block.tensor
        def _(pe):
            def lookup(i):
                pe.wait_ge(high_set, i + 1)
                pe.wait_ge(low_set, i + 1)
                if i >= 2:
                    pe.wait_ge(lookup_copied, i - 1)
                for c in range(CHUNKS_OF[i]):
                    if c < VECTOR_CHUNKS_OF[i]:
                        n = FIRST_VECTOR[i] + c
                        pe.wait_ge(one_hot_set, n + 1)
                        columns = one_hot[0:TABLE_PARTS, n % ONE_HOT_RING, :]
                    else:
                        k = c - VECTOR_CHUNKS_OF[i]
                        pe.wait_ge(scalar_one_hot_set, FIRST_SCALAR[i] + k + 1)
                        columns = scalar_one_hot[0:TABLE_PARTS, i % 2, k, :]
                    pe.matmul(layer_ps[:, i % 2, :], high[0:TABLE_PARTS, i % 2, c, :], columns,
                              start=(c == 0), stop=False)
                    last = pe.matmul(layer_ps[:, i % 2, :], low[0:TABLE_PARTS, i % 2, c, :], columns,
                                     start=False, stop=(c == CHUNKS_OF[i] - 1))
                    last.then_inc(chunk_used, 1)

            def turn(n):
                t, g = divmod(n, GROUPS_PER_TILE)
                if g == 0:
                    pe.wait_ge(side_gathered[t], 16 * SIDES)
                    sources = [dense_sb[:, t, :]] + [side_sb[:, t, i, :] for i in range(SIDES)]
                else:
                    b = t * BLOCKS_PER_TILE + g - 1
                    pe.wait_ge(mixed_gathered[b], 16 * QUAD)
                    sources = [mixed_sb[:, b * QUAD + j, :] for j in range(QUAD)]
                if n >= 2:
                    pe.wait_ge(copied[COPIER[n - 2]], copies(n - 2))
                for k, source in enumerate(sources):
                    last = pe.transpose(turn_ps[:, n % 2, k, :], source, identity[:])
                last.then_inc(group_turned, 1)

            def multiply(b):
                t, g = divmod(b, BLOCKS_PER_TILE)
                if b == 0:
                    pe.wait_ge(padding_set, 1)
                    pe.wait_ge(lookup_copied, len(LOOKUP))
                if g == 0:
                    side = t * GROUPS_PER_TILE
                    pe.wait_ge(copied[COPIER[side]], copies(side))
                pe.wait_ge(copied[COPIER[group_of(b)]], copies(group_of(b)))
                if b >= 2:
                    for keeper in kept:
                        pe.wait_ge(keeper, b - 1)
                for k in range(BLOCK_QUADS):
                    q = g * BLOCK_QUADS + k
                    last = pe.matmul(product_ps[0:QUAD * SLOTS, b % 2, k, 0:QUAD * OTHERS],
                                     turned[:, t, q, :, :].rearrange("p j f -> p (j f)"),
                                     turned[:, t, q, :, 1:FEATURES], start=True, stop=True)
                last.then_inc(block_multiplied, 1)

            def layers(i):
                start, end = BATCHES[i]
                here, wide = slice(start * P, end * P), (end - start) * P
                n = i * OUTS
                for h in range(OUTS1):
                    if n >= 2:
                        pe.wait_ge(layer_taken[n % 2], layer_turns(n - 2))
                    pe.matmul(layer_ps[:, n % 2, 0:wide], w1_sb[:, PAIR_CHUNKS, h * P:(h + 1) * P],
                              dense_turned[:, here], start=True, stop=False)
                    if h == 0:
                        for t in range(start, end):
                            pe.wait_ge(pairs_in[t], 16 * len(PAIR_LOADS))
                    for c, rows in enumerate(CHUNK_ROWS):
                        last = pe.matmul(layer_ps[:, n % 2, 0:wide], w1_sb[0:rows, c, h * P:(h + 1) * P],
                                         pairs[0:rows, c, here], start=False, stop=(c == PAIR_CHUNKS - 1))
                    last.then_inc(layer_done, 1)
                    n += 1
                for h in range(OUTS2):
                    pe.wait_ge(layer_taken[n % 2], layer_turns(n - 2))
                    for c in range(OUTS1):
                        if h == 0:
                            m = i * OUTS + c
                            pe.wait_ge(layer_taken[m % 2], layer_turns(m))
                        last = pe.matmul(layer_ps[:, n % 2, 0:wide], w2_sb[:, c, h * P:(h + 1) * P],
                                         hidden1[:, c, 0:wide], start=(c == 0), stop=(c == OUTS1 - 1))
                    last.then_inc(layer_done, 1)
                    n += 1
                for c in range(OUTS2):
                    m = i * OUTS + OUTS1 + c
                    pe.wait_ge(layer_taken[m % 2], layer_turns(m))
                    last = pe.matmul(layer_ps[0:1, n % 2, 0:wide], w3_sb[:, c:c + 1], hidden2[:, c, 0:wide],
                                     start=(c == 0), stop=(c == OUTS2 - 1))
                last.then_inc(layer_done, 1)

            pe.wait_ge(identity_set, 1)
            for _ in range(WARM_UPS):
                pe.matmul(turn_ps[:, 0, 0, :], identity[:], identity[:], start=True, stop=True)
            for step, n in PLAN:
                if step == "lookup":
                    lookup(n)
                elif step == "turn":
                    if n == 0:
                        pe.wait_ge(dense_in, 16)
                    turn(n)
                elif step == "multiply":
                    multiply(n)
                else:
                    if n == 0:
                        pe.wait_ge(w1_in, 16 * (PAIR_CHUNKS + 1))
                        pe.wait_ge(w2_in, 16)
                        pe.wait_ge(small_in, 16 * 3)
                    layers(n)

        def copy_group(copy, eng, which, n):
            if COPIER[n] != which:
                return
            t, g = divmod(n, GROUPS_PER_TILE)
            eng.wait_ge(group_turned, n + 1)
            if g == 0:
                copy(dense_turned[:, t * P:(t + 1) * P], turn_ps[:, n % 2, 0, :])
                copy(turned[:, t, :, :, 0:FIRST_LOOKUP].rearrange("p q j f -> p f j q"),
                     turn_ps[:, n % 2, 0:FIRST_LOOKUP, :].rearrange("p f (j q) -> p f j q", j=QUAD)
                     ).then_inc(copied[which], 1)
            else:
                copy(turned[:, t, (g - 1) * BLOCK_QUADS:g * BLOCK_QUADS, :, FIRST_MIXED:FEATURES
                            ].rearrange("p q j f -> p j q f"),
                     turn_ps[:, n % 2, :, :].rearrange("p j (q f) -> p j q f", f=MIXED_PER_SAMPLE)
                     ).then_inc(copied[which], 1)

        def keep(copy, eng, which, b):
            t, g = divmod(b, BLOCKS_PER_TILE)
            eng.wait_ge(block_multiplied, b + 1)
            if g == 0 and t >= 2:
                eng.wait_ge(stored[t - 2], 16 * QUAD)
            half = BLOCK_QUADS // 2
            q = g * BLOCK_QUADS + which * half
            copy(products[:, t % 2, :, :, q:q + half].rearrange("p j g q -> p q (j g)"),
                 product_ps[0:QUAD * SLOTS, b % 2, which * half:(which + 1) * half, 0:QUAD * OTHERS]
                 ).then_inc(kept[which], 1)

        def take_layers(copy, relu, eng, which, batch):
            start, end = BATCHES[batch]
            here, wide = slice(start * P, end * P), (end - start) * P
            for i in range(OUTS):
                n = batch * OUTS + i
                if n % 2 != which:
                    continue
                eng.wait_ge(layer_done, n + 1)
                source = layer_ps[:, n % 2, 0:wide]
                if i < OUTS1:
                    done = relu(hidden1[:, i, 0:wide], source, b1_sb[:, i:i + 1])
                elif i < OUTS1 + OUTS2:
                    done = relu(hidden2[:, i - OUTS1, 0:wide], source, b2_sb[:, i - OUTS1:i - OUTS1 + 1])
                else:
                    done = copy(y_sb[:, here], source[0:1, :])
                done.then_inc(layer_taken[which], 1)

        @block.vector
        def _(dve):
            def relu(dst, src, bias):
                return dve.tensor_scalar(dst, src, bias, 0.0, ALU.add, ALU.max)

            def make_one_hot(i, c):
                n = FIRST_VECTOR[i] + c
                if n >= ONE_HOT_RING:
                    table = max(m for m in range(i + 1) if FIRST_VECTOR[m] <= n - ONE_HOT_RING)
                    dve.wait_ge(chunk_used, FIRST_CHUNK[table] + n - ONE_HOT_RING - FIRST_VECTOR[table] + 1)
                kind = 1 + CHUNK_KINDS.index(CHUNKS_OF[i])
                dve.tensor_scalar(one_hot[0:TABLE_PARTS, n % ONE_HOT_RING, :],
                                  lookup_ids_sb[0:TABLE_PARTS, i % RAW_RING, :],
                                  float(-c), starts_sb[0:TABLE_PARTS, kind:kind + 1],
                                  ALU.add, ALU.is_equal).then_inc(one_hot_set, 1)

            def make_one_hots(i):
                dve.wait_ge(lookup_ids_in[i], 16)
                make_one_hot(i, 0)
                dve.wait_ge(table_in[i], 16)
                dve.wait_ge(high_set, i + 1)
                if i >= 2:
                    dve.wait_ge(chunk_used, FIRST_CHUNK[i - 1])
                size = (slice(0, TABLE_PARTS), slice(0, CHUNKS_OF[i]))
                dve.tensor_tensor(low[size[0], i % 2, size[1], :], raw[size[0], i % RAW_RING, size[1], :],
                                  high[size[0], i % 2, size[1], :].bitcast(F32), ALU.subtract
                                  ).then_inc(low_set, 1)
                for c in range(1, VECTOR_CHUNKS_OF[i]):
                    make_one_hot(i, c)

            dve.memset(turned[:, :, :, :, FEATURES:SLOTS].rearrange("p t q j f -> p (t q j) f"), 0.0
                       ).then_inc(padding_set, 1)
            dve.wait_ge(mixed_ids_in, 16)
            dve.wait_ge(starts_in, 16)
            dve.tensor_scalar(mixed_rows_sb[:], mixed_ids_sb[:], starts_sb[:, 0:1], None, ALU.add
                              ).then_inc(mixed_rows_set, 1)
            for step, n in PLAN:
                if step == "lookup":
                    make_one_hots(n)
                elif step == "turn":
                    copy_group(dve.tensor_copy, dve, 0, n)
                elif step == "multiply":
                    keep(dve.tensor_copy, dve, 0, n)
                else:
                    if n == 0:
                        dve.wait_ge(small_in, 16 * 3)
                    take_layers(dve.tensor_copy, relu, dve, 0, n)

        @block.scalar
        def _(act):
            def relu(dst, src, bias):
                return act.activation(dst, src, ACT.Relu, bias=bias)

            def round_table(i):
                act.wait_ge(table_in[i], 16)
                if i >= 2:
                    act.wait_ge(chunk_used, FIRST_CHUNK[i - 1])
                act.copy(high[0:TABLE_PARTS, i % 2, 0:CHUNKS_OF[i], :],
                         raw[0:TABLE_PARTS, i % RAW_RING, 0:CHUNKS_OF[i], :]).then_inc(high_set, 1)

            def make_one_hots(i):
                act.wait_ge(lookup_ids_in[i], 16)
                if i >= 2:
                    act.wait_ge(chunk_used, FIRST_CHUNK[i - 1])
                for k in range(SCALAR_CHUNKS_OF[i]):
                    n = FIRST_SCALAR[i] + k
                    if n >= 1:
                        act.wait_ge(scalar_one_hot_set, n)
                    act.activation(distance[0:TABLE_PARTS, :], lookup_ids_sb[0:TABLE_PARTS, i % RAW_RING, :],
                                   ACT.Square, bias=starts_sb[0:TABLE_PARTS, FIRST_START + n:FIRST_START + n + 1]
                                   ).then_inc(distance_set, 1)
                    act.wait_ge(distance_set, n + 1)
                    act.activation(scalar_one_hot[0:TABLE_PARTS, i % 2, k, :], distance[0:TABLE_PARTS, :],
                                   ACT.Relu, bias=1.0, scale=-1.0).then_inc(scalar_one_hot_set, 1)

            def copy_lookup(i):
                act.wait_ge(chunk_used, FIRST_CHUNK[i + 1])
                act.copy(turned[:, :, :, :, FIRST_LOOKUP + i].rearrange("p t q j -> p t j q"),
                         layer_ps[:, i % 2, :].rearrange("p (t j q) -> p t j q", t=TILES, j=QUAD)
                         ).then_inc(lookup_copied, 1)

            act.dma_start(mixed_ids_sb[:], mixed_ids).then_inc(mixed_ids_in, 16)
            act.dma_start(starts_sb[:], starts).then_inc(starts_in, 16)
            round_table(0)
            act.wait_ge(starts_in, 16)
            make_one_hots(0)
            round_table(1)
            make_one_hots(1)
            for step, n in PLAN:
                if step == "lookup":
                    copy_lookup(n)
                    if n + 2 < len(LOOKUP):
                        round_table(n + 2)
                        make_one_hots(n + 2)
                elif step == "turn":
                    copy_group(act.copy, act, 1, n)
                elif step == "multiply":
                    keep(act.copy, act, 1, n)
                else:
                    if n == 0:
                        act.wait_ge(small_in, 16 * 3)
                    take_layers(act.copy, relu, act, 1, n)


def kernel(**inputs):
    import numpy as np
    import concourse.bacc as bacc
    from concourse import mybir
    from concourse.bass_utils import run_bass_kernel_spmd

    nc = bacc.Bacc("TRN2", target_bir_lowering=False, num_devices=1)
    arrays = {}

    def arg(name, array):
        arrays["in_" + name] = a = np.ascontiguousarray(array)
        return nc.dram_tensor("in_" + name, a.shape, mybir.dt.from_np(a.dtype), kind="ExternalInput").ap()

    def columns(v):
        return np.asarray(v).reshape(-1, P).T

    ids = np.asarray(inputs["ids"])
    tables = [np.asarray(inputs[f"tbl_{f}"]) for f in range(TABLES)]
    mixed_ids = ids[:, MIXED].reshape(TILES, QUAD, BLOCKS_PER_TILE, BLOCK_QUADS, MIXED_PER_SAMPLE)
    mixed_ids = mixed_ids.transpose(3, 4, 0, 2, 1).reshape(P, GATHERS)
    side_ids = ids[:, SIDE].reshape(TILES, P, SIDES).transpose(1, 0, 2).reshape(P, TILES * SIDES)
    starts = np.zeros((P, FIRST_START + FIRST_SCALAR[-1]), np.float32)
    table_start = [sum(ROWS_OF[f] for f in MIXED[:i]) for i in range(MIXED_PER_SAMPLE)]
    starts[:, 0] = np.tile(np.array(table_start), BLOCK_QUADS)
    for k, chunks in enumerate(CHUNK_KINDS):
        starts[:, 1 + k] = np.arange(P) * chunks
    for i, chunks in enumerate(CHUNKS_OF):
        for k in range(SCALAR_CHUNKS_OF[i]):
            starts[:, FIRST_START + FIRST_SCALAR[i] + k] = -(np.arange(P) * chunks + VECTOR_CHUNKS_OF[i] + k)
    w1 = np.asarray(inputs["W_top1"])
    w1 = np.concatenate([w1[:PAIRS][pair_order()], w1[PAIRS:]])
    out = nc.dram_tensor("out_y", (1, BATCH), F32, kind="ExternalOutput").ap()
    dlrm_tower(
        nc, arg("dense", inputs["r_bottom_output"]),
        arg("side_ids", side_ids), [arg(f"tbl_{f}", tables[f]) for f in SIDE],
        arg("lookup_ids", ids[:, LOOKUP].T), [arg(f"tbl_{f}", tables[f]) for f in LOOKUP],
        arg("mixed_ids", mixed_ids), arg("mixed_table", np.concatenate([tables[f] for f in MIXED])),
        arg("starts", starts), arg("w1", w1), arg("b1", columns(inputs["b_top1"])),
        arg("w2", inputs["W_top2"]), arg("b2", columns(inputs["b_top2"])),
        arg("w3", columns(inputs["W_top3"])), out)
    result = run_bass_kernel_spmd(nc, [arrays], core_ids=[0])
    return np.asarray(result.results[0]["out_y"]).reshape(BATCH, 1)
```

```python
from contextlib import ExitStack

import numpy as np
import concourse.bass as bass
from concourse import mybir

F32 = mybir.dt.float32
F32R = mybir.dt.float32r
I32 = mybir.dt.int32
ALU = mybir.AluOpType
ACT = mybir.ActivationFunctionType

P = 128
BATCH = 512
TILES = BATCH // P
ROWS_OF = [1000, 1250, 125000, 12500, 12500, 1000, 1000, 12500, 12500, 1250, 12500, 1250, 12500,
           1250, 1250, 1250, 1000, 1000, 1250, 1250, 12500, 1000, 1250, 1250, 12500, 1250]
TABLES = len(ROWS_OF)
FEATURES = TABLES + 1
SLOTS = 28
QUAD = 4
QUADS = P // QUAD

MIXED_PER_SAMPLE = 16
SIDES = 2
BY_SIZE = sorted(range(TABLES), key=lambda f: ROWS_OF[f])
LOOKUP = BY_SIZE[:TABLES - MIXED_PER_SAMPLE - SIDES]
SIDE = BY_SIZE[len(LOOKUP):len(LOOKUP) + SIDES]
MIXED = BY_SIZE[len(LOOKUP) + SIDES:]
SLOT_TABLES = [None] + SIDE + LOOKUP + MIXED
FIRST_LOOKUP = 1 + SIDES
FIRST_MIXED = FIRST_LOOKUP + len(LOOKUP)

TABLE_PARTS = 125
CHUNKS_OF = [ROWS_OF[f] // TABLE_PARTS for f in LOOKUP]
MOST_CHUNKS = max(CHUNKS_OF)
CHUNK_KINDS = sorted(set(CHUNKS_OF))
FIRST_CHUNK = [sum(CHUNKS_OF[:i]) for i in range(len(LOOKUP) + 1)]
RAW_RING = 3
SCALAR_CHUNKS_OF = [1] * len(LOOKUP)
SCALAR_CHUNKS = max(SCALAR_CHUNKS_OF)
VECTOR_CHUNKS_OF = [c - s for c, s in zip(CHUNKS_OF, SCALAR_CHUNKS_OF)]
FIRST_SCALAR = [sum(SCALAR_CHUNKS_OF[:i]) for i in range(len(LOOKUP) + 1)]
FIRST_VECTOR = [sum(VECTOR_CHUNKS_OF[:i]) for i in range(len(LOOKUP) + 1)]
FIRST_START = 1 + len(CHUNK_KINDS)
ONE_HOT_RING = 4
WARM_UPS = 14

BANK = 512
GATHER_QUADS = P // MIXED_PER_SAMPLE // QUAD
GATHERS = BATCH // QUAD // GATHER_QUADS
TILE_GATHERS = GATHERS // TILES
FULL = 4
GATHERS_OF = [FULL] * (GATHERS // FULL - 1) + [3, 1]
BLOCKS = len(GATHERS_OF)
FIRST_GATHER = [sum(GATHERS_OF[:b]) for b in range(BLOCKS + 1)]

SPAN = 13
OTHERS = FEATURES - 1
ROWS = SLOTS * OTHERS

PARTS = [(0, 4), (4, 8), (8, 12), (12, 17)]
EARLY_PARTS = 2
LATE_BLOCK = 9
LATE_ORDER = "ot m ot m oo m to to m oo to m o to m t o t m m oo"

HIDDEN1, HIDDEN2 = 512, 256
OUTS1, OUTS2 = HIDDEN1 // P, HIDDEN2 // P
OUTS = OUTS1 + OUTS2 + 1

PER_CHUNK = 4
SPARE = P - PER_CHUNK * OTHERS
PAIR_LOADS = [(0, OTHERS * i, i, OTHERS, 3, PER_CHUNK, FEATURES) for i in range(PER_CHUNK)]
PAIR_LOADS += [(0, PER_CHUNK * OTHERS, SPAN - 1, SPARE, 1, 0, FEATURES),
               (1, PER_CHUNK * OTHERS, SPAN - 1 + SPARE * FEATURES, OTHERS - SPARE, 1, 0, FEATURES),
               (2, PER_CHUNK * OTHERS, SPAN, SPAN, 1, 0, 1)]
LAST_PART = len(PARTS) - 1
POOL_STORES, POOL_LOADS = [QUAD - 1], PAIR_LOADS[-2:]
CHUNK_ROWS = [P, PER_CHUNK * OTHERS + OTHERS - SPARE, PER_CHUNK * OTHERS + SPAN]
PAIR_CHUNKS = len(CHUNK_ROWS)
CHUNK_START = [sum(CHUNK_ROWS[:c]) for c in range(PAIR_CHUNKS + 1)]
PAIRS = CHUNK_START[-1]

TURN_BANKS, PRODUCT_BANKS, LAYER_BANKS = [0, 1], [2, 3, 4, 5], [6, 7]

def tile_of(b):
    return FIRST_GATHER[b] // TILE_GATHERS


def quads_of(b):
    first = FIRST_GATHER[b] - tile_of(b) * TILE_GATHERS
    return slice(first * GATHER_QUADS, (first + GATHERS_OF[b]) * GATHER_QUADS)


GROUPS = []
for tile in range(TILES):
    GROUPS.append(("side", tile))
    GROUPS += [("block", b) for b in range(BLOCKS) if tile_of(b) == tile]


def group_of(b):
    return GROUPS.index(("block", b))


def plan():
    steps, turned = [], 0

    def turn_up_to(n):
        nonlocal turned
        while turned <= min(n, len(GROUPS) - 1):
            steps.append(("turn", turned))
            turned += 1

    for i in range(len(LOOKUP)):
        steps.append(("lookup", i))
        if i >= 2:
            turn_up_to(i - 2)
    turn_up_to(len(LOOKUP) - 2)
    for b in range(LATE_BLOCK):
        turn_up_to(group_of(b + 1))
        steps.append(("multiply", b))
    late = {"t": ("turn", turned), "m": ("multiply", LATE_BLOCK), "o": ("output", 0)}
    for letter in LATE_ORDER.replace(" ", ""):
        steps.append(late[letter])
        late[letter] = (late[letter][0], late[letter][1] + 1)
    assert [n for _, n in late.values()] == [len(GROUPS), BLOCKS, EARLY_PARTS * OUTS]
    steps += [("layers", p) for p in range(EARLY_PARTS, len(PARTS))]
    return steps


PLAN = plan()
LAST_LOOKUP = PLAN.index(("lookup", len(LOOKUP) - 1))
COPIER = [1 if PLAN.index(("turn", n)) <= LAST_LOOKUP else n % 2 for n in range(len(GROUPS))]


def copies(n):
    return COPIER[:n + 1].count(COPIER[n])


def layer_turns(n):
    return n // 2 + 1


def bank_of(n):
    part, k = divmod(n, OUTS)
    if part < EARLY_PARTS:
        return LAYER_BANKS[n % 2]
    return (PRODUCT_BANKS + LAYER_BANKS + TURN_BANKS)[k]


def bank_user(n):
    return max((m for m in range(n) if bank_of(m) == bank_of(n)), default=None)


def columns_of(p):
    first, end = PARTS[p]
    return slice(*(FIRST_GATHER[b] * GATHER_QUADS * QUAD for b in (first, end)))


def width(p):
    return columns_of(p).stop - columns_of(p).start


def tile_and_quads(p):
    first, end = PARTS[p]
    return tile_of(first), slice(quads_of(first).start, quads_of(end - 1).stop)


def hardware_stores(p):
    return [j for j in range(QUAD) if p < LAST_PART or j not in POOL_STORES]


def sync_loads(p):
    return [load for load in PAIR_LOADS if p < LAST_PART or load not in POOL_LOADS]


def pair_order():
    number = {}
    for f in range(FEATURES):
        for g in range(f + 1, FEATURES):
            number[f, g] = len(number)
    feature = [0] + [f + 1 for f in SLOT_TABLES[1:]]
    order = np.zeros(PAIRS, np.int64)
    for chunk, part, row, rows, chunks, chunk_step, step in PAIR_LOADS:
        for c in range(chunks):
            for r in range(rows):
                f, g = divmod(row + c * chunk_step + r * step, OTHERS)
                f, g = feature[f], feature[g + 1]
                order[CHUNK_START[chunk + c] + part + r] = number[min(f, g), max(f, g)]
    assert sorted(order) == list(range(len(number)))
    return order


def dlrm_tower(nc, dense, side_ids, side_tables, lookup_ids, lookup_tables, mixed_ids, mixed_table, starts,
               w1, b1, w2, b2, w3, out):
    with ExitStack() as ctx:
        def sb(name, shape, dt=F32):
            return ctx.enter_context(nc.sbuf_tensor(name, shape, dt))

        def psum(name, shape):
            return ctx.enter_context(nc.psum_tensor(name, shape, F32))

        def sem(name):
            return ctx.enter_context(nc.semaphore(name))

        starts_sb = sb("starts_sb", [P, FIRST_START + FIRST_SCALAR[-1]])
        mixed_ids_sb = sb("mixed_ids_sb", [P, GATHERS], I32)
        mixed_rows_sb = sb("mixed_rows_sb", [P, GATHERS], I32)
        side_ids_sb = sb("side_ids_sb", [P, TILES, SIDES], I32)
        lookup_ids_sb = sb("lookup_ids_sb", [P, RAW_RING, BATCH], I32)
        identity = sb("identity", [P, P])
        side_sb = sb("side_sb", [P, TILES, SIDES, P])
        mixed_sb = sb("mixed_sb", [P, GATHERS, P])
        raw = sb("raw", [P, RAW_RING, MOST_CHUNKS, P])
        high = sb("high", [P, 2, MOST_CHUNKS, P], F32R)
        low = sb("low", [P, 2, MOST_CHUNKS, P], F32R)
        one_hot = sb("one_hot", [P, ONE_HOT_RING, BATCH], F32R)
        scalar_one_hot = sb("scalar_one_hot", [P, 2, SCALAR_CHUNKS, BATCH], F32R)
        distance = sb("distance", [P, BATCH])
        turned = sb("turned", [P, TILES, QUADS, QUAD, SLOTS])
        dense_turned = sb("dense_turned", [P, BATCH])
        products = sb("products", [QUAD * SLOTS, 2, QUAD, OTHERS, QUADS])
        pairs = sb("pairs", [P, PAIR_CHUNKS, BATCH])
        w1_sb = sb("w1_sb", [P, PAIR_CHUNKS + 1, HIDDEN1])
        w2_sb = sb("w2_sb", [P, OUTS1, HIDDEN2])
        w3_sb = sb("w3_sb", [P, OUTS2])
        b1_sb = sb("b1_sb", [P, OUTS1])
        b2_sb = sb("b2_sb", [P, OUTS2])
        hidden1 = sb("hidden1", [P, OUTS1, P])
        hidden2 = sb("hidden2", [P, OUTS2, P])
        y_sb = sb("y_sb", [1, BATCH])
        products_dram = nc.dram_tensor("products_dram", (ROWS * BATCH,), F32, kind="Internal").ap()

        banks = psum("banks", [P, 8, BANK])
        turn_ps = banks[:, TURN_BANKS[0]:TURN_BANKS[-1] + 1, :].rearrange("p b (k d) -> p b k d", k=QUAD)
        product_ps = banks[:, PRODUCT_BANKS[0]:PRODUCT_BANKS[-1] + 1, :].rearrange(
            "p (two b) (k d) -> p two b k d", two=2, d=P)
        lookup_ps = banks[:, LAYER_BANKS[0]:LAYER_BANKS[-1] + 1, :]

        starts_in, mixed_ids_in, side_ids_in = sem("starts_in"), sem("mixed_ids_in"), sem("side_ids_in")
        lookup_ids_in = [sem(f"lookup_ids_in_{i}") for i in range(len(LOOKUP))]
        table_in = [sem(f"table_in_{i}") for i in range(len(LOOKUP))]
        dense_in, dense_spread, w1_in, w2_in, small_in = sem("dense_in"), sem("dense_spread"), sem("w1_in"), sem("w2_in"), sem("small_in")
        ones_set, identity_set, padding_set = sem("ones_set"), sem("identity_set"), sem("padding_set")
        mixed_rows_set = sem("mixed_rows_set")
        side_gathered = [sem(f"side_gathered_{t}") for t in range(TILES)]
        mixed_gathered = [sem(f"mixed_gathered_{b}") for b in range(BLOCKS)]
        high_set, low_set = sem("high_set"), sem("low_set")
        one_hot_set, scalar_one_hot_set, distance_set = sem("one_hot_set"), sem("scalar_one_hot_set"), sem("distance_set")
        chunk_used = sem("chunk_used")
        lookup_copied = sem("lookup_copied")
        group_turned = sem("group_turned")
        copied = [sem("copied_by_vector"), sem("copied_by_scalar")]
        block_multiplied = sem("block_multiplied")
        kept = [sem("kept_by_vector"), sem("kept_by_scalar")]
        stored = [sem(f"stored_{p}") for p in range(len(PARTS))]
        pairs_in = [sem(f"pairs_in_{p}") for p in range(len(PARTS))]
        stored_by_pool, pairs_in_by_pool = sem("stored_by_pool"), sem("pairs_in_by_pool")
        layer_done = sem("layer_done")
        layer_taken = [sem("layer_taken_by_vector"), sem("layer_taken_by_scalar")]
        y_stored = sem("y_stored")

        block = ctx.enter_context(nc.Block())

        def store_part(eng, p, samples, signal):
            for keeper in kept:
                eng.wait_ge(keeper, PARTS[p][1])
            t, quads = tile_and_quads(p)
            n = quads.stop - quads.start
            start = ROWS * columns_of(p).start
            for j in samples:
                eng.dma_start(
                    bass.AP(products_dram.tensor, start + j * n,
                            [[OTHERS * width(p), SLOTS], [width(p), OTHERS], [1, n]]),
                    products[j * SLOTS:(j + 1) * SLOTS, t % 2, j, :, quads]).then_inc(signal, 16)

        def load_part(eng, p, loads, signal):
            eng.wait_ge(stored[p], 16 * len(hardware_stores(p)))
            if p == LAST_PART:
                eng.wait_ge(stored_by_pool, 16 * len(POOL_STORES))
            start = ROWS * columns_of(p).start
            for chunk, part, row, rows, chunks, chunk_step, step in loads:
                eng.dma_start(pairs[part:part + rows, chunk:chunk + chunks, columns_of(p)],
                              bass.AP(products_dram.tensor, start + row * width(p),
                                      [[step * width(p), rows], [chunk_step * width(p), chunks], [1, width(p)]])
                              ).then_inc(signal, 16)

        @block.gpsimd
        def _(pool):
            pool.memset(identity[:], 1.0).then_inc(ones_set, 1)
            pool.wait_ge(ones_set, 1)
            pool.affine_select(out=identity[:], in_=identity[:], compare_op=ALU.is_equal, fill=0.0, base=0,
                               pattern=[[-1, P]], channel_multiplier=1).then_inc(identity_set, 1)
            for t in range(TILES):
                if t == 0:
                    pool.wait_ge(side_ids_in, 16)
                for i in range(SIDES):
                    pool.indirect_dma_start(
                        side_sb[:, t, i, :], None, side_tables[i],
                        bass.IndirectOffsetOnAxis(ap=side_ids_sb[:, t, i:i + 1], axis=0),
                    ).then_inc(side_gathered[t], 16)
                if t == 0:
                    pool.wait_ge(mixed_rows_set, 1)
                for b in [b for b in range(BLOCKS) if tile_of(b) == t]:
                    for n in range(FIRST_GATHER[b], FIRST_GATHER[b + 1]):
                        pool.indirect_dma_start(
                            mixed_sb[:, n, :], None, mixed_table,
                            bass.IndirectOffsetOnAxis(ap=mixed_rows_sb[:, n:n + 1], axis=0),
                        ).then_inc(mixed_gathered[b], 16)
            store_part(pool, LAST_PART, POOL_STORES, stored_by_pool)
            load_part(pool, LAST_PART, POOL_LOADS, pairs_in_by_pool)

        @block.sync
        def _(sp):
            def load_table(i):
                sp.dma_start(raw[0:TABLE_PARTS, i % RAW_RING, 0:CHUNKS_OF[i], :].rearrange("p c d -> p (c d)"),
                             lookup_tables[i].rearrange("(p c) d -> p (c d)", p=TABLE_PARTS)
                             ).then_inc(table_in[i], 16)

            def load_lookup_ids(i):
                sp.dma_start(lookup_ids_sb[:, i % RAW_RING, :], lookup_ids[i:i + 1, :].to_broadcast([P, BATCH])
                             ).then_inc(lookup_ids_in[i], 16)

            sp.dma_start(side_ids_sb[:].rearrange("p t i -> p (t i)"), side_ids).then_inc(side_ids_in, 16)
            load_table(0)
            load_lookup_ids(0)
            sp.dma_start(dense_turned[:], dense).then_inc(dense_in, 16)
            for i in range(1, RAW_RING):
                load_table(i)
                load_lookup_ids(i)
            for i in range(RAW_RING, len(LOOKUP)):
                sp.wait_ge(high_set, i - RAW_RING + 1)
                sp.wait_ge(low_set, i - RAW_RING + 1)
                load_table(i)
                sp.wait_ge(one_hot_set, FIRST_VECTOR[i - RAW_RING + 1])
                sp.wait_ge(distance_set, FIRST_SCALAR[i - RAW_RING + 1])
                load_lookup_ids(i)
            for c, rows in enumerate(CHUNK_ROWS + [P]):
                start = sum(CHUNK_ROWS[:c])
                sp.dma_start(w1_sb[0:rows, c, :], w1[start:start + rows, :]).then_inc(w1_in, 16)
            sp.dma_start(w2_sb[:], w2.rearrange("(c p) n -> p c n", p=P)).then_inc(w2_in, 16)
            sp.dma_start(w3_sb[:], w3).then_inc(small_in, 16)
            sp.dma_start(b1_sb[:], b1).then_inc(small_in, 16)
            sp.dma_start(b2_sb[:], b2).then_inc(small_in, 16)
            for p in range(len(PARTS)):
                if p < LAST_PART:
                    store_part(sp, p, hardware_stores(p), stored[p])
                load_part(sp, p, sync_loads(p), pairs_in[p])
            for which in range(2):
                n = len(PARTS) * OUTS - 1 - which
                sp.wait_ge(layer_taken[n % 2], layer_turns(n))
            sp.dma_start(out, y_sb[:]).then_inc(y_stored, 16)
            sp.wait_ge(y_stored, 16)

        @block.tensor
        def _(pe):
            def lookup(i):
                pe.wait_ge(high_set, i + 1)
                pe.wait_ge(low_set, i + 1)
                if i >= 2:
                    pe.wait_ge(lookup_copied, i - 1)
                for c in range(CHUNKS_OF[i]):
                    if c < VECTOR_CHUNKS_OF[i]:
                        n = FIRST_VECTOR[i] + c
                        pe.wait_ge(one_hot_set, n + 1)
                        columns = one_hot[0:TABLE_PARTS, n % ONE_HOT_RING, :]
                    else:
                        k = c - VECTOR_CHUNKS_OF[i]
                        pe.wait_ge(scalar_one_hot_set, FIRST_SCALAR[i] + k + 1)
                        columns = scalar_one_hot[0:TABLE_PARTS, i % 2, k, :]
                    pe.matmul(lookup_ps[:, i % 2, :], high[0:TABLE_PARTS, i % 2, c, :], columns,
                              start=(c == 0), stop=False)
                    last = pe.matmul(lookup_ps[:, i % 2, :], low[0:TABLE_PARTS, i % 2, c, :], columns,
                                     start=False, stop=(c == CHUNKS_OF[i] - 1))
                    last.then_inc(chunk_used, 1)

            def turn(n):
                kind, m = GROUPS[n]
                if kind == "side":
                    pe.wait_ge(side_gathered[m], 16 * SIDES)
                    sources = [side_sb[:, m, i, :] for i in range(SIDES)]
                else:
                    pe.wait_ge(mixed_gathered[m], 16 * GATHERS_OF[m])
                    sources = [mixed_sb[:, i, :] for i in range(FIRST_GATHER[m], FIRST_GATHER[m + 1])]
                if n >= 2:
                    pe.wait_ge(copied[COPIER[n - 2]], copies(n - 2))
                for k, source in enumerate(sources):
                    last = pe.transpose(turn_ps[:, n % 2, k, :], source, identity[:])
                last.then_inc(group_turned, 1)

            def multiply(b):
                t, quads, half = tile_of(b), quads_of(b), GATHERS_OF[b] * GATHER_QUADS // 2
                if b == 0:
                    pe.wait_ge(padding_set, 1)
                    pe.wait_ge(dense_spread, 1)
                    pe.wait_ge(lookup_copied, len(LOOKUP))
                if b == 0 or tile_of(b - 1) < t:
                    side = GROUPS.index(("side", t))
                    pe.wait_ge(copied[COPIER[side]], copies(side))
                pe.wait_ge(copied[COPIER[group_of(b)]], copies(group_of(b)))
                if b >= 2:
                    for keeper in kept:
                        pe.wait_ge(keeper, b - 1)
                for k in range(2 * half):
                    q = quads.start + k
                    last = pe.matmul(product_ps[0:QUAD * SLOTS, b % 2, k // half, k % half, 0:QUAD * OTHERS],
                                     turned[:, t, q, :, :].rearrange("p j f -> p (j f)"),
                                     turned[:, t, q, :, 1:FEATURES], start=True, stop=True)
                last.then_inc(block_multiplied, 1)

            def out(n, rows=P):
                return banks[0:rows, bank_of(n), 0:width(n // OUTS)]

            def open_bank(n):
                if bank_user(n) is not None:
                    pe.wait_ge(layer_taken[bank_user(n) % 2], layer_turns(bank_user(n)))
                elif bank_of(n) in TURN_BANKS:
                    group = len(GROUPS) - 2 + (len(GROUPS) + bank_of(n)) % 2
                    pe.wait_ge(copied[COPIER[group]], copies(group))
                elif bank_of(n) in PRODUCT_BANKS:
                    for keeper in kept:
                        pe.wait_ge(keeper, BLOCKS)

            def await_taken(n):
                pe.wait_ge(layer_taken[n % 2], layer_turns(n))

            def await_pairs(p):
                pe.wait_ge(pairs_in[p], 16 * len(sync_loads(p)))
                if p == LAST_PART:
                    pe.wait_ge(pairs_in_by_pool, 16 * len(POOL_LOADS))

            def add_dense(n):
                p, h = divmod(n, OUTS)
                t, quads = tile_and_quads(p)
                samples = dense_turned[:, t * P:(t + 1) * P].rearrange("d (j q) -> d j q", j=QUAD)[:, :, quads]
                pe.matmul(out(n).rearrange("h (j q) -> h j q", j=QUAD), w1_sb[:, PAIR_CHUNKS, h * P:(h + 1) * P],
                          samples, start=True, stop=False)

            def add_pairs(n):
                p, h = divmod(n, OUTS)
                for c, rows in enumerate(CHUNK_ROWS):
                    last = pe.matmul(out(n), w1_sb[0:rows, c, h * P:(h + 1) * P], pairs[0:rows, c, columns_of(p)],
                                     start=False, stop=(c == PAIR_CHUNKS - 1))
                return last

            def add_hidden1(n, c):
                p, k = divmod(n, OUTS)
                h = k - OUTS1
                return pe.matmul(out(n), w2_sb[:, c, h * P:(h + 1) * P], hidden1[:, c, 0:width(p)],
                                 start=(c == 0), stop=(c == OUTS1 - 1))

            def y(n):
                p = n // OUTS
                for c in range(OUTS2):
                    await_taken(p * OUTS + OUTS1 + c)
                    last = pe.matmul(out(n, 1), w3_sb[:, c:c + 1], hidden2[:, c, 0:width(p)],
                                     start=(c == 0), stop=(c == OUTS2 - 1))
                return last

            def output(n):
                p, k = divmod(n, OUTS)
                open_bank(n)
                if k < OUTS1:
                    add_dense(n)
                    await_pairs(p)
                    last = add_pairs(n)
                elif k < OUTS1 + OUTS2:
                    for c in range(OUTS1):
                        await_taken(p * OUTS + c)
                        last = add_hidden1(n, c)
                else:
                    last = y(n)
                last.then_inc(layer_done, 1)

            def layers(p):
                first = p * OUTS
                for n in range(first, first + OUTS1):
                    open_bank(n)
                    add_dense(n)
                await_pairs(p)
                for n in range(first, first + OUTS1):
                    add_pairs(n).then_inc(layer_done, 1)
                for n in range(first + OUTS1, first + OUTS1 + OUTS2):
                    open_bank(n)
                    for c in range(OUTS1 - 1):
                        await_taken(first + c)
                        add_hidden1(n, c)
                await_taken(first + OUTS1 - 1)
                for n in range(first + OUTS1, first + OUTS1 + OUTS2):
                    add_hidden1(n, OUTS1 - 1).then_inc(layer_done, 1)
                open_bank(first + OUTS - 1)
                y(first + OUTS - 1).then_inc(layer_done, 1)

            pe.wait_ge(identity_set, 1)
            for _ in range(WARM_UPS):
                pe.matmul(turn_ps[:, 0, 0, :], identity[:], identity[:], start=True, stop=True)
            for step, n in PLAN:
                if step == "lookup":
                    lookup(n)
                elif step == "turn":
                    turn(n)
                elif step == "multiply":
                    multiply(n)
                elif step == "output":
                    if n == 0:
                        pe.wait_ge(dense_in, 16)
                        pe.wait_ge(w1_in, 16 * (PAIR_CHUNKS + 1))
                        pe.wait_ge(w2_in, 16)
                        pe.wait_ge(small_in, 16 * 3)
                    output(n)
                else:
                    layers(n)

        def copy_group(copy, eng, which, n):
            if COPIER[n] != which:
                return
            kind, m = GROUPS[n]
            eng.wait_ge(group_turned, n + 1)
            if kind == "side":
                copy(turned[:, m, :, :, 1:FIRST_LOOKUP].rearrange("p q j f -> p f j q"),
                     turn_ps[:, n % 2, 0:SIDES, :].rearrange("p f (j q) -> p f j q", j=QUAD)
                     ).then_inc(copied[which], 1)
            else:
                copy(turned[:, tile_of(m), quads_of(m), :, FIRST_MIXED:FEATURES],
                     turn_ps[:, n % 2, 0:GATHERS_OF[m], :].rearrange("p i (q j f) -> p (i q) j f", q=GATHER_QUADS,
                                                                     j=QUAD)
                     ).then_inc(copied[which], 1)

        def keep(copy, eng, which, b):
            t, half = tile_of(b), GATHERS_OF[b] * GATHER_QUADS // 2
            eng.wait_ge(block_multiplied, b + 1)
            if t >= 2 and tile_of(b - 1) < t:
                eng.wait_ge(stored[t - 2], 16 * len(hardware_stores(t - 2)))
            q = quads_of(b).start + which * half
            copy(products[:, t % 2, :, :, q:q + half].rearrange("p j g q -> p q (j g)"),
                 product_ps[0:QUAD * SLOTS, b % 2, which, 0:half, 0:QUAD * OTHERS]
                 ).then_inc(kept[which], 1)

        def take_output(copy, relu, eng, which, n):
            if n % 2 != which:
                return
            p, k = divmod(n, OUTS)
            eng.wait_ge(layer_done, n + 1)
            source = banks[:, bank_of(n), 0:width(p)]
            if k < OUTS1:
                done = relu(hidden1[:, k, 0:width(p)], source, b1_sb[:, k:k + 1])
            elif k < OUTS1 + OUTS2:
                done = relu(hidden2[:, k - OUTS1, 0:width(p)], source, b2_sb[:, k - OUTS1:k - OUTS1 + 1])
            else:
                t, quads = tile_and_quads(p)
                done = copy(y_sb[:, t * P:(t + 1) * P].rearrange("o (j q) -> o j q", j=QUAD)[:, :, quads],
                            source[0:1, :].rearrange("o (j q) -> o j q", j=QUAD))
            done.then_inc(layer_taken[which], 1)

        @block.vector
        def _(dve):
            def relu(dst, src, bias):
                return dve.tensor_scalar(dst, src, bias, 0.0, ALU.add, ALU.max)

            def make_one_hot(i, c):
                n = FIRST_VECTOR[i] + c
                if n >= ONE_HOT_RING:
                    table = max(m for m in range(i + 1) if FIRST_VECTOR[m] <= n - ONE_HOT_RING)
                    dve.wait_ge(chunk_used, FIRST_CHUNK[table] + n - ONE_HOT_RING - FIRST_VECTOR[table] + 1)
                kind = 1 + CHUNK_KINDS.index(CHUNKS_OF[i])
                dve.tensor_scalar(one_hot[0:TABLE_PARTS, n % ONE_HOT_RING, :],
                                  lookup_ids_sb[0:TABLE_PARTS, i % RAW_RING, :],
                                  float(-c), starts_sb[0:TABLE_PARTS, kind:kind + 1],
                                  ALU.add, ALU.is_equal).then_inc(one_hot_set, 1)

            def make_one_hots(i):
                dve.wait_ge(lookup_ids_in[i], 16)
                make_one_hot(i, 0)
                dve.wait_ge(table_in[i], 16)
                dve.wait_ge(high_set, i + 1)
                if i >= 2:
                    dve.wait_ge(chunk_used, FIRST_CHUNK[i - 1])
                size = (slice(0, TABLE_PARTS), slice(0, CHUNKS_OF[i]))
                dve.tensor_tensor(low[size[0], i % 2, size[1], :], raw[size[0], i % RAW_RING, size[1], :],
                                  high[size[0], i % 2, size[1], :].bitcast(F32), ALU.subtract
                                  ).then_inc(low_set, 1)
                for c in range(1, VECTOR_CHUNKS_OF[i]):
                    make_one_hot(i, c)

            dve.memset(turned[:, :, :, :, FEATURES:SLOTS].rearrange("p t q j f -> p (t q j) f"), 0.0
                       ).then_inc(padding_set, 1)
            dve.wait_ge(mixed_ids_in, 16)
            dve.wait_ge(starts_in, 16)
            dve.tensor_scalar(mixed_rows_sb[:], mixed_ids_sb[:], starts_sb[:, 0:1], None, ALU.add
                              ).then_inc(mixed_rows_set, 1)
            for step, n in PLAN:
                if step == "lookup":
                    make_one_hots(n)
                elif step == "turn":
                    copy_group(dve.tensor_copy, dve, 0, n)
                elif step == "multiply":
                    keep(dve.tensor_copy, dve, 0, n)
                elif step == "output":
                    if n == 0:
                        dve.wait_ge(small_in, 16 * 3)
                    take_output(dve.tensor_copy, relu, dve, 0, n)
                else:
                    for k in range(OUTS):
                        take_output(dve.tensor_copy, relu, dve, 0, n * OUTS + k)

        @block.scalar
        def _(act):
            def relu(dst, src, bias):
                return act.activation(dst, src, ACT.Relu, bias=bias)

            def round_table(i):
                act.wait_ge(table_in[i], 16)
                if i >= 2:
                    act.wait_ge(chunk_used, FIRST_CHUNK[i - 1])
                act.copy(high[0:TABLE_PARTS, i % 2, 0:CHUNKS_OF[i], :],
                         raw[0:TABLE_PARTS, i % RAW_RING, 0:CHUNKS_OF[i], :]).then_inc(high_set, 1)

            def make_one_hots(i):
                act.wait_ge(lookup_ids_in[i], 16)
                if i >= 2:
                    act.wait_ge(chunk_used, FIRST_CHUNK[i - 1])
                for k in range(SCALAR_CHUNKS_OF[i]):
                    n = FIRST_SCALAR[i] + k
                    if n >= 1:
                        act.wait_ge(scalar_one_hot_set, n)
                    act.activation(distance[0:TABLE_PARTS, :], lookup_ids_sb[0:TABLE_PARTS, i % RAW_RING, :],
                                   ACT.Square, bias=starts_sb[0:TABLE_PARTS, FIRST_START + n:FIRST_START + n + 1]
                                   ).then_inc(distance_set, 1)
                    act.wait_ge(distance_set, n + 1)
                    act.activation(scalar_one_hot[0:TABLE_PARTS, i % 2, k, :], distance[0:TABLE_PARTS, :],
                                   ACT.Relu, bias=1.0, scale=-1.0).then_inc(scalar_one_hot_set, 1)

            def copy_lookup(i):
                act.wait_ge(chunk_used, FIRST_CHUNK[i + 1])
                act.copy(turned[:, :, :, :, FIRST_LOOKUP + i].rearrange("p t q j -> p t j q"),
                         lookup_ps[:, i % 2, :].rearrange("p (t j q) -> p t j q", t=TILES, j=QUAD)
                         ).then_inc(lookup_copied, 1)

            act.dma_start(mixed_ids_sb[:], mixed_ids).then_inc(mixed_ids_in, 16)
            act.dma_start(starts_sb[:], starts).then_inc(starts_in, 16)
            round_table(0)
            act.wait_ge(starts_in, 16)
            make_one_hots(0)
            round_table(1)
            make_one_hots(1)
            act.wait_ge(dense_in, 16)
            act.copy(turned[:, :, :, :, 0].rearrange("p t q j -> p t j q"),
                     dense_turned[:].rearrange("p (t j q) -> p t j q", t=TILES, j=QUAD)).then_inc(dense_spread, 1)
            for step, n in PLAN:
                if step == "lookup":
                    copy_lookup(n)
                    if n + 2 < len(LOOKUP):
                        round_table(n + 2)
                        make_one_hots(n + 2)
                elif step == "turn":
                    copy_group(act.copy, act, 1, n)
                elif step == "multiply":
                    keep(act.copy, act, 1, n)
                    if n == BLOCKS - 1:
                        store_part(act, LAST_PART, hardware_stores(LAST_PART), stored[LAST_PART])
                elif step == "output":
                    if n == 0:
                        act.wait_ge(small_in, 16 * 3)
                    take_output(act.copy, relu, act, 1, n)
                else:
                    for k in range(OUTS):
                        take_output(act.copy, relu, act, 1, n * OUTS + k)


def kernel(**inputs):
    import numpy as np
    import concourse.bacc as bacc
    from concourse import mybir
    from concourse.bass_utils import run_bass_kernel_spmd

    nc = bacc.Bacc("TRN2", target_bir_lowering=False, num_devices=1)
    arrays = {}

    def arg(name, array):
        arrays["in_" + name] = a = np.ascontiguousarray(array)
        return nc.dram_tensor("in_" + name, a.shape, mybir.dt.from_np(a.dtype), kind="ExternalInput").ap()

    def columns(v):
        return np.asarray(v).reshape(-1, P).T

    ids = np.asarray(inputs["ids"])
    tables = [np.asarray(inputs[f"tbl_{f}"]) for f in range(TABLES)]
    mixed_ids = ids[:, MIXED].reshape(TILES, QUAD, TILE_GATHERS, GATHER_QUADS, MIXED_PER_SAMPLE)
    mixed_ids = mixed_ids.transpose(3, 1, 4, 0, 2).reshape(P, GATHERS)
    side_ids = ids[:, SIDE].reshape(TILES, P, SIDES).transpose(1, 0, 2).reshape(P, TILES * SIDES)
    starts = np.zeros((P, FIRST_START + FIRST_SCALAR[-1]), np.float32)
    table_start = [sum(ROWS_OF[f] for f in MIXED[:i]) for i in range(MIXED_PER_SAMPLE)]
    starts[:, 0] = np.tile(np.array(table_start), GATHER_QUADS * QUAD)
    for k, chunks in enumerate(CHUNK_KINDS):
        starts[:, 1 + k] = np.arange(P) * chunks
    for i, chunks in enumerate(CHUNKS_OF):
        for k in range(SCALAR_CHUNKS_OF[i]):
            starts[:, FIRST_START + FIRST_SCALAR[i] + k] = -(np.arange(P) * chunks + VECTOR_CHUNKS_OF[i] + k)
    w1 = np.asarray(inputs["W_top1"])
    w1 = np.concatenate([w1[:PAIRS][pair_order()], w1[PAIRS:]])
    out = nc.dram_tensor("out_y", (1, BATCH), F32, kind="ExternalOutput").ap()
    dlrm_tower(
        nc, arg("dense", np.asarray(inputs["r_bottom_output"]).T),
        arg("side_ids", side_ids), [arg(f"tbl_{f}", tables[f]) for f in SIDE],
        arg("lookup_ids", ids[:, LOOKUP].T), [arg(f"tbl_{f}", tables[f]) for f in LOOKUP],
        arg("mixed_ids", mixed_ids), arg("mixed_table", np.concatenate([tables[f] for f in MIXED])),
        arg("starts", starts), arg("w1", w1), arg("b1", columns(inputs["b_top1"])),
        arg("w2", inputs["W_top2"]), arg("b2", columns(inputs["b_top2"])),
        arg("w3", columns(inputs["W_top3"])), out)
    result = run_bass_kernel_spmd(nc, [arrays], core_ids=[0])
    return np.asarray(result.results[0]["out_y"]).reshape(BATCH, 1)
```
